# Optimizing a Trainium2 kernel written in Bass

```python
import numpy as np
import jax
import jax.numpy as jnp

def _softmax(x, axis=-1):
    return jax.nn.softmax(x, axis=axis)

def _gelu(x):
    return jax.nn.gelu(x, approximate=True)

def _silu(x):
    return jax.nn.silu(x)

def _sigmoid(x):
    return jax.nn.sigmoid(x)

def _layernorm(x, axis=-1, eps=1e-05):
    m = jnp.mean(x, axis=axis, keepdims=True)
    v = jnp.var(x, axis=axis, keepdims=True)
    return (x - m) / jnp.sqrt(v + eps)

def _scatter_add(tgt, idx, src, axis=0):
    return tgt.at[idx].add(src)

def _segment_sum(src, seg, n):
    return jax.ops.segment_sum(src, seg, n)
kernel_name = 'mk_xattn_ffn_d2_seqx_r8_d462a8'

def setup_inputs(seed: int=0):
    np.random.seed(seed)
    _w = jnp.asarray

    def _rec_inputs():
        import jax
        import jax.numpy as jnp
        _rk = jax.random.key(seed)
        x = -0.0002928 + 1 * jax.random.normal(jax.random.fold_in(_rk, 1), (16, 128, 128), jnp.float32)
        _lenS = 128 - jax.random.randint(jax.random.fold_in(_rk, 7), (16,), 0, max(1, 128 // 4) + 1, jnp.int32)
        _lenS2 = 128 - jax.random.randint(jax.random.fold_in(_rk, 8), (16,), 0, max(1, 128 // 4) + 1, jnp.int32)
        _ctx_1024P = jax.random.normal(jax.random.fold_in(_rk, 11), (16, 16, 128), jnp.float32)
        _ctx_1024c = jax.random.dirichlet(jax.random.fold_in(_rk, 511), 0.3 * jnp.ones((16,), jnp.float32), (16, 128))
        _ctx_1024t = jnp.einsum('bsk,bkd->bsd', _ctx_1024c, _ctx_1024P)
        _ctx_1024t = _ctx_1024t * jax.lax.rsqrt(jnp.mean(jnp.square(_ctx_1024t)) + 1e-12) * 0.953939
        ctx_1024 = -1.39393e-06 + 0.999914 * (_ctx_1024t + 0.3 * jax.random.normal(jax.random.fold_in(_rk, 611), (16, 128, 128), jnp.float32))
        return (x, ctx_1024)
    x, ctx_1024 = _rec_inputs()

    def _L0_xattn_setup():
        import jax, jax.numpy as jnp
        import numpy as np
        D_MODEL = 128
        HEADS = 16
        DK = D_MODEL // HEADS
        DV = D_MODEL // HEADS
        key = jax.random.key(seed)
        ks = jax.random.split(key, 8)
        N, S = (2, 256)
        Q = jax.random.normal(ks[0], (N, S, D_MODEL), dtype=jnp.float32)
        K = jax.random.normal(ks[1], (N, S, D_MODEL), dtype=jnp.float32)
        V = jax.random.normal(ks[2], (N, S, D_MODEL), dtype=jnp.float32)
        sc = 1.0 / np.sqrt(D_MODEL)
        WQ = jax.random.normal(ks[3], (HEADS * DK, D_MODEL), dtype=jnp.float32) * sc
        WK = jax.random.normal(ks[4], (HEADS * DK, D_MODEL), dtype=jnp.float32) * sc
        WV = jax.random.normal(ks[5], (HEADS * DV, D_MODEL), dtype=jnp.float32) * sc
        WO = jax.random.normal(ks[6], (D_MODEL, HEADS * DV), dtype=jnp.float32) * sc
        bO = jax.random.normal(ks[7], (D_MODEL,), dtype=jnp.float32) * 0.01
        return {'Q': Q, 'K': K, 'V': V, 'WQ': WQ, 'WK': WK, 'WV': WV, 'WO': WO, 'bO': bO}
    _L0_xattn_all = _L0_xattn_setup()
    _L0_xattn_in = {k: v for k, v in _L0_xattn_all.items() if k in ('WQ', 'WK', 'WV', 'WO', 'bO')}
    del _L0_xattn_all

    def _L0_ffn_setup():
        import jax, jax.numpy as jnp
        import numpy as np
        B, F, D, H, E, K = (4, 256, 128, 256, 8, 2)
        key = jax.random.key(seed)
        ks = jax.random.split(key, 9)
        sc = lambda k, shape, fan_in: jax.random.normal(k, shape, jnp.float32) * fan_in ** (-0.5)
        return {'x': jax.random.normal(ks[0], (B, F, D), jnp.float32), 'rw1': sc(ks[1], (D, D), D), 'rb1': jnp.zeros((D,), jnp.float32), 'rw2': sc(ks[2], (D, E), D), 'rb2': jnp.zeros((E,), jnp.float32), 'ew1': sc(ks[3], (E, D, H), D), 'eb1': jnp.zeros((E, H), jnp.float32), 'ew2': sc(ks[4], (E, H, D), H), 'eb2': jnp.zeros((E, D), jnp.float32)}
    _L0_ffn_all = _L0_ffn_setup()
    _L0_ffn_in = {k: v for k, v in _L0_ffn_all.items() if k in ('rw1', 'rb1', 'rw2', 'rb2', 'ew1', 'eb1', 'ew2', 'eb2')}
    del _L0_ffn_all

    def _L1_xattn_setup():
        import jax, jax.numpy as jnp
        import numpy as np
        E = 128
        H = 16
        HD = E // H
        BASE = 10000.0

        def _rope_cache(seq_len):
            inv_freq = 1.0 / BASE ** (jnp.arange(0, HD, 2, dtype=jnp.float32) / HD)
            t = jnp.arange(seq_len, dtype=jnp.float32)
            freqs = jnp.einsum('i,j->ij', t, inv_freq)
            emb = jnp.concatenate([freqs, freqs], axis=-1)
            return (jnp.cos(emb)[None, None], jnp.sin(emb)[None, None])

        def _rotate_half(x):
            x1, x2 = (x[..., :HD // 2], x[..., HD // 2:])
            return jnp.concatenate([-x2, x1], axis=-1)

        def _apply_rope(x, cos, sin):
            return x * cos + _rotate_half(x) * sin
        key = jax.random.key(seed)
        ks = jax.random.split(key, 11)
        B, S = (2, 256)
        std = 1.0 / np.sqrt(E)
        inp = {'query': jax.random.normal(ks[0], (B, S, E), dtype=jnp.float32), 'key': jax.random.normal(ks[1], (B, S, E), dtype=jnp.float32), 'value': jax.random.normal(ks[2], (B, S, E), dtype=jnp.float32), 'Wq': jax.random.normal(ks[3], (E, E), dtype=jnp.float32) * std, 'bq': jnp.zeros((E,), dtype=jnp.float32), 'Wk': jax.random.normal(ks[4], (E, E), dtype=jnp.float32) * std, 'bk': jnp.zeros((E,), dtype=jnp.float32), 'Wv': jax.random.normal(ks[5], (E, E), dtype=jnp.float32) * std, 'bv': jnp.zeros((E,), dtype=jnp.float32), 'Wo': jax.random.normal(ks[6], (E, E), dtype=jnp.float32) * std, 'bo': jnp.zeros((E,), dtype=jnp.float32)}
        return inp
    _L1_xattn_all = _L1_xattn_setup()
    _L1_xattn_in = {k: v for k, v in _L1_xattn_all.items() if k in ('Wq', 'bq', 'Wk', 'bk', 'Wv', 'bv', 'Wo', 'bo')}
    del _L1_xattn_all

    def _L1_ffn_setup():
        import jax, jax.numpy as jnp
        import numpy as np
        B, T, C, H, E, MIN_E = (4, 256, 128, 128, 16, 2)
        IS_CAUSAL = False

        def _forward(hidden_states, sim_matrix, gates, q_proj, k_proj, v_proj, o_proj):
            b, t, c = hidden_states.shape
            n = b * t
            x = hidden_states.reshape(n, c)
            xn = x / jnp.maximum(jnp.linalg.norm(x, axis=-1, keepdims=True), 1e-12)
            sn = sim_matrix / jnp.maximum(jnp.linalg.norm(sim_matrix, axis=0, keepdims=True), 1e-12)
            logits = xn @ sn - jax.nn.sigmoid(gates)
            gated = jax.nn.relu(logits)
            hard = (gated > 0).astype(gated.dtype)
            mask = gated + jax.lax.stop_gradient(hard - gated)
            inactive = jnp.sum(hard, axis=1) == 0
            _, fb_idx = jax.lax.top_k(logits, MIN_E)
            fb = jnp.zeros((n, logits.shape[1]), gated.dtype).at[jnp.arange(n)[:, None], fb_idx].set(1.0)
            put = jax.lax.stop_gradient(inactive[:, None].astype(gated.dtype) * fb)
            mask = mask * (1.0 - put) + put
            masked = jnp.where(mask > 0, gated, -jnp.inf)
            w = jax.nn.softmax(masked, axis=-1)

            def moe_proj(p):
                y = jnp.einsum('nc,ech->neh', x, p)
                return jnp.einsum('ne,neh->nh', w, y)
            q = moe_proj(q_proj).reshape(b, t, -1)
            k = moe_proj(k_proj).reshape(b, t, -1)
            v = moe_proj(v_proj).reshape(b, t, -1)
            h = q.shape[-1]
            scores = jnp.einsum('bth,bsh->bts', q, k) / jnp.sqrt(jnp.asarray(h, q.dtype))
            if IS_CAUSAL and t > 1:
                causal = jnp.tril(jnp.ones((t, t), bool))
                scores = jnp.where(causal[None], scores, -jnp.inf)
            attn = jax.nn.softmax(scores, axis=-1)
            o = jnp.einsum('bts,bsh->bth', attn, v).reshape(n, h)
            z = jnp.einsum('ne,nh->enh', w, o)
            out = jnp.einsum('enh,ehc->nc', z, o_proj)
            return out.reshape(b, t, c)
        key = jax.random.key(seed)
        ks = jax.random.split(key, 6)
        lim_qkv = float(np.sqrt(6.0 / (C + H)))
        inp = {'hidden_states': jax.random.normal(ks[0], (B, T, C), jnp.float32), 'sim_matrix': jax.random.normal(ks[1], (C, E), jnp.float32), 'gates': jnp.zeros((E,), jnp.float32), 'q_proj': jax.random.uniform(ks[2], (E, C, H), jnp.float32, -lim_qkv, lim_qkv), 'k_proj': jax.random.uniform(ks[3], (E, C, H), jnp.float32, -lim_qkv, lim_qkv), 'v_proj': jax.random.uniform(ks[4], (E, C, H), jnp.float32, -lim_qkv, lim_qkv), 'o_proj': jax.random.uniform(ks[5], (E, H, C), jnp.float32, -lim_qkv, lim_qkv)}
        return inp
    _L1_ffn_all = _L1_ffn_setup()
    _L1_ffn_in = {k: v for k, v in _L1_ffn_all.items() if k in ('sim_matrix', 'gates', 'q_proj', 'k_proj', 'v_proj', 'o_proj')}
    del _L1_ffn_all
    return {'x': x, 'ctx_1024': ctx_1024, 'L0_xattn_WQ': _L0_xattn_in['WQ'], 'L0_xattn_WK': _L0_xattn_in['WK'], 'L0_xattn_WV': _L0_xattn_in['WV'], 'L0_xattn_WO': _L0_xattn_in['WO'], 'L0_xattn_bO': _L0_xattn_in['bO'], 'L0_ffn_rw1': _L0_ffn_in['rw1'], 'L0_ffn_rb1': _L0_ffn_in['rb1'], 'L0_ffn_rw2': _L0_ffn_in['rw2'], 'L0_ffn_rb2': _L0_ffn_in['rb2'], 'L0_ffn_ew1': _L0_ffn_in['ew1'], 'L0_ffn_eb1': _L0_ffn_in['eb1'], 'L0_ffn_ew2': _L0_ffn_in['ew2'], 'L0_ffn_eb2': _L0_ffn_in['eb2'], 'L1_xattn_Wq': _L1_xattn_in['Wq'], 'L1_xattn_bq': _L1_xattn_in['bq'], 'L1_xattn_Wk': _L1_xattn_in['Wk'], 'L1_xattn_bk': _L1_xattn_in['bk'], 'L1_xattn_Wv': _L1_xattn_in['Wv'], 'L1_xattn_bv': _L1_xattn_in['bv'], 'L1_xattn_Wo': _L1_xattn_in['Wo'], 'L1_xattn_bo': _L1_xattn_in['bo'], 'L1_ffn_sim_matrix': _L1_ffn_in['sim_matrix'], 'L1_ffn_gates': _L1_ffn_in['gates'], 'L1_ffn_q_proj': _L1_ffn_in['q_proj'], 'L1_ffn_k_proj': _L1_ffn_in['k_proj'], 'L1_ffn_v_proj': _L1_ffn_in['v_proj'], 'L1_ffn_o_proj': _L1_ffn_in['o_proj']}

def reference(x, ctx_1024, L0_xattn_WQ, L0_xattn_WK, L0_xattn_WV, L0_xattn_WO, L0_xattn_bO, L0_ffn_rw1, L0_ffn_rb1, L0_ffn_rw2, L0_ffn_rb2, L0_ffn_ew1, L0_ffn_eb1, L0_ffn_ew2, L0_ffn_eb2, L1_xattn_Wq, L1_xattn_bq, L1_xattn_Wk, L1_xattn_bk, L1_xattn_Wv, L1_xattn_bv, L1_xattn_Wo, L1_xattn_bo, L1_ffn_sim_matrix, L1_ffn_gates, L1_ffn_q_proj, L1_ffn_k_proj, L1_ffn_v_proj, L1_ffn_o_proj):
    import jax
    import jax.numpy as jnp

    def _L0_xattn_ref(Q, K, V, WQ, WK, WV, WO, bO):
        import jax, jax.numpy as jnp
        import numpy as np
        D_MODEL = 128
        HEADS = 16
        DK = D_MODEL // HEADS
        DV = D_MODEL // HEADS
        N, ql, _ = Q.shape
        kl = K.shape[1]
        q = (Q @ WQ.T).reshape(N, ql, HEADS, DK)
        k = (K @ WK.T).reshape(N, kl, HEADS, DK)
        v = (V @ WV.T).reshape(N, kl, HEADS, DV)
        compat = jnp.einsum('nqhk,nlhk->nhql', q, k) / jnp.sqrt(jnp.float32(DK))
        causal = jnp.tril(jnp.ones((ql, kl), dtype=bool))
        compat = jnp.where(causal, compat, -jnp.inf)
        weights = jax.nn.softmax(compat, axis=3)
        attn = jnp.einsum('nhqk,nkhv->nqhv', weights, v).reshape(N, ql, HEADS * DV)
        return attn @ WO.T + bO

    def _L0_ffn_ref(x, rw1, rb1, rw2, rb2, ew1, eb1, ew2, eb2):
        import jax, jax.numpy as jnp
        import numpy as np
        B, F, D, H, E, K = (4, 256, 128, 256, 8, 2)
        b, f, d = x.shape
        t = x.reshape(b * f, d)
        logits = jax.nn.silu(t @ rw1 + rb1) @ rw2 + rb2
        vals, idx = jax.lax.top_k(logits, K)
        rows = jnp.arange(t.shape[0])[:, None]
        masked = jnp.full_like(logits, -jnp.inf).at[rows, idx].set(vals)
        w = jax.nn.softmax(masked, axis=1)
        eh = jax.nn.silu(jnp.einsum('td,edh->teh', t, ew1) + eb1[None])
        eo = jnp.einsum('teh,ehd->ted', eh, ew2) + eb2[None]
        y = t + jnp.einsum('te,ted->td', w, eo)
        return y.reshape(b, f, d)

    def _L1_xattn_ref(query, key, value, Wq, bq, Wk, bk, Wv, bv, Wo, bo):
        import jax, jax.numpy as jnp
        import numpy as np
        E = 128
        H = 16
        HD = E // H
        BASE = 10000.0

        def _rope_cache(seq_len):
            inv_freq = 1.0 / BASE ** (jnp.arange(0, HD, 2, dtype=jnp.float32) / HD)
            t = jnp.arange(seq_len, dtype=jnp.float32)
            freqs = jnp.einsum('i,j->ij', t, inv_freq)
            emb = jnp.concatenate([freqs, freqs], axis=-1)
            return (jnp.cos(emb)[None, None], jnp.sin(emb)[None, None])

        def _rotate_half(x):
            x1, x2 = (x[..., :HD // 2], x[..., HD // 2:])
            return jnp.concatenate([-x2, x1], axis=-1)

        def _apply_rope(x, cos, sin):
            return x * cos + _rotate_half(x) * sin
        B, Sq, _ = query.shape
        Sk = key.shape[1]
        Q = query @ Wq.T + bq
        K = key @ Wk.T + bk
        V = value @ Wv.T + bv
        Q = Q.reshape(B, Sq, H, HD).transpose(0, 2, 1, 3)
        K = K.reshape(B, Sk, H, HD).transpose(0, 2, 1, 3)
        V = V.reshape(B, Sk, H, HD).transpose(0, 2, 1, 3)
        cos_q, sin_q = _rope_cache(Sq)
        cos_k, sin_k = _rope_cache(Sk)
        Q = _apply_rope(_apply_rope(Q, cos_q, sin_q), cos_q, sin_q)
        K = _apply_rope(_apply_rope(K, cos_k, sin_k), cos_k, sin_k)
        scale = 1.0 / jnp.sqrt(jnp.float32(HD))
        scores = jnp.einsum('bhqd,bhkd->bhqk', Q, K) * scale
        weights = jax.nn.softmax(scores, axis=-1)
        out = jnp.einsum('bhqk,bhkd->bhqd', weights, V)
        out = out.transpose(0, 2, 1, 3).reshape(B, Sq, E)
        return out @ Wo.T + bo

    def _L1_ffn_ref(hidden_states, sim_matrix, gates, q_proj, k_proj, v_proj, o_proj):
        import jax, jax.numpy as jnp
        import numpy as np
        B, T, C, H, E, MIN_E = (4, 256, 128, 128, 16, 2)
        IS_CAUSAL = False

        def _forward(hidden_states, sim_matrix, gates, q_proj, k_proj, v_proj, o_proj):
            b, t, c = hidden_states.shape
            n = b * t
            x = hidden_states.reshape(n, c)
            xn = x / jnp.maximum(jnp.linalg.norm(x, axis=-1, keepdims=True), 1e-12)
            sn = sim_matrix / jnp.maximum(jnp.linalg.norm(sim_matrix, axis=0, keepdims=True), 1e-12)
            logits = xn @ sn - jax.nn.sigmoid(gates)
            gated = jax.nn.relu(logits)
            hard = (gated > 0).astype(gated.dtype)
            mask = gated + jax.lax.stop_gradient(hard - gated)
            inactive = jnp.sum(hard, axis=1) == 0
            _, fb_idx = jax.lax.top_k(logits, MIN_E)
            fb = jnp.zeros((n, logits.shape[1]), gated.dtype).at[jnp.arange(n)[:, None], fb_idx].set(1.0)
            put = jax.lax.stop_gradient(inactive[:, None].astype(gated.dtype) * fb)
            mask = mask * (1.0 - put) + put
            masked = jnp.where(mask > 0, gated, -jnp.inf)
            w = jax.nn.softmax(masked, axis=-1)

            def moe_proj(p):
                y = jnp.einsum('nc,ech->neh', x, p)
                return jnp.einsum('ne,neh->nh', w, y)
            q = moe_proj(q_proj).reshape(b, t, -1)
            k = moe_proj(k_proj).reshape(b, t, -1)
            v = moe_proj(v_proj).reshape(b, t, -1)
            h = q.shape[-1]
            scores = jnp.einsum('bth,bsh->bts', q, k) / jnp.sqrt(jnp.asarray(h, q.dtype))
            if IS_CAUSAL and t > 1:
                causal = jnp.tril(jnp.ones((t, t), bool))
                scores = jnp.where(causal[None], scores, -jnp.inf)
            attn = jax.nn.softmax(scores, axis=-1)
            o = jnp.einsum('bts,bsh->bth', attn, v).reshape(n, h)
            z = jnp.einsum('ne,nh->enh', w, o)
            out = jnp.einsum('enh,ehc->nc', z, o_proj)
            return out.reshape(b, t, c)
        return _forward(hidden_states, sim_matrix, gates, q_proj, k_proj, v_proj, o_proj)
    x = x + _L0_xattn_ref(_layernorm(x, axis=-1), ctx_1024, ctx_1024, L0_xattn_WQ, L0_xattn_WK, L0_xattn_WV, L0_xattn_WO, L0_xattn_bO)
    x = x + _L0_ffn_ref(_layernorm(x, axis=-1), L0_ffn_rw1, L0_ffn_rb1, L0_ffn_rw2, L0_ffn_rb2, L0_ffn_ew1, L0_ffn_eb1, L0_ffn_ew2, L0_ffn_eb2)
    x = x + _L1_xattn_ref(_layernorm(x, axis=-1), ctx_1024, ctx_1024, L1_xattn_Wq, L1_xattn_bq, L1_xattn_Wk, L1_xattn_bk, L1_xattn_Wv, L1_xattn_bv, L1_xattn_Wo, L1_xattn_bo)
    x = x + _L1_ffn_ref(_layernorm(x, axis=-1), L1_ffn_sim_matrix, L1_ffn_gates, L1_ffn_q_proj, L1_ffn_k_proj, L1_ffn_v_proj, L1_ffn_o_proj)
    return x

_drawn_inputs = setup_inputs


def setup_inputs(seed=0):
    import zlib

    import numpy as np

    out = dict(_drawn_inputs(seed))
    spreads = {'L0_ffn_rb1': (0.0, 0.1),
     'L0_ffn_rb2': (0.0, 0.1),
     'L0_ffn_eb1': (0.0, 0.393),
     'L0_ffn_eb2': (0.0, 0.1),
     'L1_xattn_bq': (0.0, 0.733),
     'L1_xattn_bk': (0.0, 0.8),
     'L1_xattn_bv': (0.0, 0.1),
     'L1_xattn_bo': (0.0, 0.1),
     'L1_ffn_gates': (0.0, 0.1)}
    factors = {'L0_xattn_bO': 3.839, 'L1_ffn_q_proj': 4.505, 'L1_ffn_k_proj': 4.52}
    for name, (base, spread) in spreads.items():
        noise = np.random.default_rng([zlib.crc32(name.encode()), seed]).standard_normal(out[name].shape)
        drawn = base * np.exp(spread * noise) if base else spread * noise
        out[name] = jnp.asarray(drawn.astype(out[name].dtype))
    for name, factor in factors.items():
        out[name] = (out[name] * factor).astype(out[name].dtype)
    return out
```

```python
import concourse.bass as bass
from concourse import mybir
from contextlib import ExitStack
import numpy as np

F32, F32R, BF16, U32 = mybir.dt.float32, mybir.dt.float32r, mybir.dt.bfloat16, mybir.dt.uint32
ALU = mybir.AluOpType
ACT = mybir.ActivationFunctionType
AX = mybir.AxisListType

B, S, D = 16, 128, 128
H, HD = 16, 8
KD = 4
QUADS, PER = 4, 4
SLOTS = 32
NEGMAX = 24
E0, H0 = 8, 256
HC = H0 // 128
E1 = 16
G, GT = 4, 4
GW = GT * S
EPS = 1e-5
TINY = 1e-24
SCALE = HD ** -0.5
SCALE1 = D ** -0.5


def r2(ap):
    return ap.bitcast(F32)


class Core:

    def __init__(self, nc, ctx):
        self.nc, self.ctx, self.phases = nc, ctx, 0
        self.bank = [ctx.enter_context(nc.psum_tensor(f"bank{i}", [128, 512], F32)) for i in range(8)]
        self.rooms = ctx.enter_context(ExitStack())
        self.x = self.sb("x_res", [128, B, D])

    def sb(self, name, shape, dt=F32):
        return self.ctx.enter_context(self.nc.sbuf_tensor(name, shape, dt))

    def room(self):
        self.rooms.close()
        return lambda name, shape, dt=F32: self.rooms.enter_context(
            self.nc.sbuf_tensor(f"{name}_{self.phases}", shape, dt))

    def sem(self, name):
        one = self.nc.alloc_semaphore(name=name)
        self.sems.append(one)
        return one

    def phase(self, build, a):
        self.sems = []
        self.phases += 1
        PASSED.append(self.sem(f"passed{self.phases}"))
        build(self.nc, self, a)
        self.nc.clear_and_free_semaphores(self.sems)
        self.nc.all_engine_barrier()


def chain(eng, sem):
    count = [0]

    def link(ins):
        count[0] += 1
        ins.then_inc(sem, 1)
        eng.wait_ge(sem, count[0])
    return link


PASSED = []


def stand(eng, sem, value):
    eng.wait_ge(sem, value)
    eng.sem_inc(PASSED[-1], 1)


def setup(nc, k, a):
    sb, sem = k.sb, k.sem
    k.ident = sb("ident", [128, 128])
    k.identr = sb("identr", [128, 128], F32R)
    k.identb = sb("identb", [128, 128], BF16)
    k.mask_qk = sb("mask_qk", [128, PER, S], BF16)
    k.ones_row = sb("ones_row", [1, 128])
    k.ones = sb("ones", [128, 128])
    k.iota = sb("iota", [128, E1])
    k.sel0 = sb("sel0", [128, E0, 128], F32R)
    k.sel1 = sb("sel1", [128, E1, 128], F32R)
    k.mhalf = sb("mhalf", [128, B])
    k.rope = sb("rope", [128, 2, HD])
    k.wq, k.wkv, k.wo, k.bq, k.bkv, k.bo = [], [], [], [], [], []
    loads = [(k.x[:], a["x"]), (k.ident[:], a["c_ident"]),
             (k.iota[:], a["c_iota"]), (k.rope[:], a["c_rope"])]
    for n in range(2):
        k.wq.append(sb(f"wq{n}", [128, 128]))
        k.wkv.append(sb(f"wkv{n}", [128, 256]))
        k.wo.append(sb(f"wo{n}", [128, 128]))
        k.bo.append(sb(f"bo{n}", [128, 128]))
        loads += [(k.wq[n][:], a[f"wqT{n}"]), (k.wkv[n][:, 0:128], a[f"wkT{n}"]),
                  (k.wkv[n][:, 128:256], a[f"wvT{n}"]), (k.wo[n][:], a[f"woT{n}"]), (k.bo[n][:], a[f"bo{n}"].partition_broadcast(128))]
    k.bq = sb("bq", [128, 128])
    k.bkv = sb("bkv", [128, 256])
    k.rw1 = sb("rw1", [128, 128])
    k.rb1 = sb("rb1", [128, 1])
    k.rw2 = sb("rw2", [128, E0])
    k.rb2 = sb("rb2", [1, E0])
    k.ew1 = sb("ew1", [128, E0, H0])
    k.eb1 = sb("eb1", [128, E0, HC])
    k.ew2 = sb("ew2", [128, E0, HC, D])
    k.eb2 = sb("eb2", [128, D])
    k.sim = sb("sim", [128, E1])
    k.gates = sb("gates", [128, E1])
    k.p1 = [sb(f"proj{n}", [128, E1, 128]) for n in range(4)]
    loads += [(k.bq[:], a["bq"].partition_broadcast(128)), (k.bkv[:, 0:128], a["bk"].partition_broadcast(128)), (k.bkv[:, 128:256], a["bv"].partition_broadcast(128)),
              (k.rw1[:], a["rw1"]), (k.rb1[:], a["rb1"]), (k.rw2[:], a["rw2"]),
              (k.rb2[:], a["rb2"]), (k.ew1[:], a["ew1"]),
              (k.eb1[:], a["eb1"]),
              (k.ew2[:], a["ew2"]), (k.eb2[0:E0, :], a["eb2"]), (k.eb2[E0:2 * E0, :], a["eb2"]),
              (k.sim[:], a["sim"]), (k.gates[:], a["gates"].partition_broadcast(128))]
    loads += [(k.p1[n][:], a[f"proj{n}"]) for n in range(4)]
    k.sn = sb("sn", [128, E1])
    k.sig = sb("sig", [128, E1])
    sq, nrm = sb("sim_sq", [128, E1]), sb("sim_nrm", [128, 2, E1])
    s_load, s_pool, s_c = sem("setup_load"), sem("setup_pool"), sem("setup_dve")
    s_sq, s_n2, s_n2c, s_rn, s_e = (sem(n) for n in ("sim_sq_r", "sim_n2", "sim_n2c", "sim_rn", "gate_exp"))
    passing = k.ctx.enter_context(ExitStack())
    raw = passing.enter_context(nc.sbuf_tensor("raw", [128, PER * S], F32))
    raws = passing.enter_context(nc.sbuf_tensor("raws", [128, (E0 + E1) * 128], F32))
    loads += [(raw[:], a["c_mask"]), (raws[:], a["c_sel"])]
    with nc.Block() as block:
        @block.sync
        def _(sp):
            for dst, src in loads:
                sp.dma_start(dst, src).then_inc(s_load, 16)
            sp.wait_ge(s_load, 16 * len(loads))

        @block.gpsimd
        def _(pool):
            pool.memset(k.ones[:], 1.0).then_inc(s_pool, 1)
            pool.memset(k.ones_row[:], 1.0).then_inc(s_pool, 1)
            pool.memset(k.mhalf[:], -0.5).then_inc(s_pool, 1)
            pool.wait_ge(s_pool, 3)
            pool.wait_ge(s_n2c, 1)
            pool.tensor_tensor(nrm[:, 1, :], nrm[:, 0, :], k.mhalf[:, 0:E1], ALU.pow).then_inc(s_rn, 1)

        @block.vector
        def _(dve):
            dve.wait_ge(s_load, 16 * len(loads))
            link = chain(dve, s_c)
            dve.tensor_tensor(sq[:], k.sim[:], k.sim[:], ALU.mult).then_inc(s_sq, 1)
            link(dve.tensor_copy(k.identr[:], k.ident[:]))
            link(dve.tensor_copy(k.identb[:], k.ident[:]))
            link(dve.tensor_copy(k.mask_qk[:], raw[:]))
            link(dve.tensor_copy(k.sel0[:], raws[:, 0:E0 * 128]))
            link(dve.tensor_copy(k.sel1[:], raws[:, E0 * 128:]))
            dve.wait_ge(s_n2, 1)
            dve.tensor_scalar(nrm[:, 0, :], k.bank[0][:, 0:E1], TINY, None, ALU.max).then_inc(s_n2c, 1)
            dve.wait_ge(s_rn, 1)
            link(dve.tensor_tensor(k.sn[:], k.sim[:], nrm[:, 1, :], ALU.mult))
            dve.wait_ge(s_e, 1)
            link(dve.tensor_scalar(k.sig[:], k.sig[:], 1.0, None, ALU.add))
            link(dve.reciprocal(k.sig[:], k.sig[:]))

        @block.scalar
        def _(act):
            act.wait_ge(s_load, 16 * len(loads))
            act.activation(k.sig[:], k.gates[:], ACT.Exp, scale=-1.0).then_inc(s_e, 1)

        @block.tensor
        def _(pe):
            pe.wait_ge(s_pool, 3)
            pe.wait_ge(s_sq, 1)
            pe.matmul(k.bank[0][:, 0:E1], k.ones[:], sq[:], start=True, stop=True).then_inc(s_n2, 1)

    passing.close()
    k.xn = sb("xn", [128, 2, D])
    k.xnT = sb("xnT", [128, 2, S])
    k.stat = sb("stat", [128, 2, 6])
    k.mv = sb("mv", [128, 2, 2])
    k.rstd = sb("rstd", [128, 2, 1])
    k.kpad = [sb(f"kpad{n}", [128, H, SLOTS], F32R) for n in range(2)]
    k.qpad = [sb(f"qpad{n}", [128, H, SLOTS], F32R) for n in range(2)]
    k.kexp = [sb(f"kexp{n}", [128, QUADS, PER, S], F32R) for n in range(2)]
    k.q2exp = [sb(f"q2exp{n}", [128, QUADS, PER, S], F32R) for n in range(2)]
    k.vaug = [sb(f"vaug{n}", [128, H, SLOTS]) for n in range(2)]
    k.on = sb("on", [128, 2, D])
    k.ot = sb("ot", [128, 2, S])
    k.var = sb("var", [128, B, 1])
    s_z = sem("zeroed")
    with nc.Block() as block:
        @block.gpsimd
        def _(pool):
            for n in range(2):
                pool.memset(r2(k.kpad[n][:]), 0.0).then_inc(s_z, 1)
                pool.memset(r2(k.qpad[n][:]), 0.0).then_inc(s_z, 1)
                pool.memset(k.vaug[n][:], 0.0).then_inc(s_z, 1)
            pool.wait_ge(s_z, 6)
            for n in range(2):
                pool.memset(r2(k.kpad[n][:, :, NEGMAX:NEGMAX + 2]), 1.0).then_inc(s_z, 1)
                pool.memset(k.vaug[n][:, :, HD], 1.0).then_inc(s_z, 1)
            pool.wait_ge(s_z, 10)

        @block.vector
        def _(dve):
            for n in range(2):
                dve.memset(r2(k.kexp[n][:]), 0.0)
                dve.memset(r2(k.q2exp[n][:]), 0.0)


def attention_room(k):
    sb = k.room()
    k.ctxc = sb("ctxc", [128, 2, S])
    k.qraw = sb("qraw", [128, 2, D])
    k.kvraw = sb("kvraw", [128, 2, 2 * D])
    k.pve = sb("pve", [128, 2, QUADS * S])
    k.rt = sb("rope_tmp", [128, 2, 2, D])
    k.kd = [sb(f"kd{n}", [128, QUADS, S], F32R) for n in range(KD)]
    k.q1 = [sb(f"q1{n}", [128, QUADS, S], F32R) for n in range(2)]
    k.q2 = [sb(f"q2{n}", [128, QUADS, S], F32R) for n in range(2)]
    k.pt = [sb(f"pt{n}", [128, PER, S]) for n in range(QUADS)]
    k.negm = sb("negm", [128, 2, H])
    k.rden = sb("rden", [128, 2, H])


def ffn_room(k):
    sb = k.room()
    k.tT = sb("tT", [128, B, S])
    k.wT = sb("wT", [128, B * S], F32R)
    k.wpad = sb("wpad", [128, B, 128], F32R)
    k.lg = [sb("logits0", [128, B, E0]), sb("logits1", [128, B, E1])]
    k.ex, k.sel, k.tmp = (sb(s, [128, B, E1]) for s in ("ex", "chosen", "tmp"))
    k.mx, k.idx = sb("mx", [128, B, 8]), sb("idx", [128, B, 8], U32)
    k.rn = sb("rn", [128, 2, B])
    k.hs = [sb(f"hs{n}", [128, GW]) for n in range(2)]
    k.hw = [sb(f"hw{n}", [128, GW]) for n in range(2)]
    k.yT, k.oT = sb("yT", [128, GW]), sb("oT", [128, GW])
    k.qkv = [sb(f"qkv{n}", [128, GW]) for n in range(3)]
    k.nm4 = sb("nm4", [128, 3 * GT])


def attention(nc, k, a, n):
    attention_room(k)
    rope = n == 1
    ctxT = a["ctxT"]
    IN, TK, TQ, SC, ST, PV = k.bank[0], k.bank[1], k.bank[2], k.bank[3:5], k.bank[5:7], k.bank[7]
    sem = lambda s: k.sem(f"L{n}_{s}")
    (xn_r, kv_r, kvc_r, xt_r, xtc_r, q_r, qc_r, kpad_r, ktr_r, kd_r, qpad_r, qtr_r, q1_r, vaug_r,
     s_r, max_r, slot_r, rez_r, q2tr_r, q2_r, st_r, exp_r, prob_r, pv_r, pvc_r, otr_r, on_r, ot_r, otc_r, op_r,
     res_r, var_r, rstd_r, kspin_r, khi_r, qspin_r, qhi_r, den_r, slot0_r, stat_r, bias_r, bo_r, qbias_r) = map(sem, (
        "xn", "kv", "kv_copied", "xT", "xT_copied", "q", "q_copied", "kpad", "k_turned", "kd",
        "qpad", "q_turned", "q1", "vaug", "scores", "max", "slots", "rezeroed", "q2_turned", "q2",
        "scoresT", "exp", "probs", "pv", "pv_copied", "pv_turned", "o", "oT", "oT_copied", "outproj",
        "residual", "var", "rstd", "k_spun", "k_high", "q_spun", "q_high", "den", "slot0", "stat", "k_bias", "x_bias", "q_bias"))
    kexp_r = [sem(f"kexp{m}") for m in range(2)]
    ctx_in = [sem(f"ctx_in{m}") for m in range(2)]
    q2exp_r = [sem(f"q2exp{m}") for m in range(2)]
    if n:
        prob_r = exp_r

    def early(b, by=2):
        return isinstance(b, int) and b < by

    def steps(eng, step):
        for b in range(-1, KD):
            step(b, b % KD)
        with eng.Fori(1, B // KD - 1) as i:
            for m in range(KD):
                step(i * KD + m, m)
        for b in range(B - KD, B + 2):
            step(b, b % KD)

    def isin(b):
        return not isinstance(b, int) or 0 <= b < B

    with nc.Block() as block:
        @block.sync
        def _(sp):
            def load_ctx(b, par):
                if not early(b):
                    stand(sp, kv_r, b - 1)
                sp.dma_start(k.ctxc[:, par, :], ctxT[:, bass.ds(b * S, S)]).then_inc(ctx_in[par], 16)

            def apart(dst, src, done):
                for j in range(PER):
                    rows = slice(SLOTS * j, SLOTS * (j + 1))
                    sp.dma_start(r2(dst[rows, :, j, :]), r2(src[rows, :, :])).then_inc(done, 16)

            def step(b, m):
                par, p, pp = m % 2, b + 1, 1 - m % 2
                if isin(b + 2):
                    load_ctx(b + 2, par)
                if isin(p):
                    stand(sp, kd_r, p + 1)
                    if not early(p):
                        sp.wait_ge(s_r, QUADS * (p - 1))
                    apart(k.kexp[pp], k.kd[(m + 1) % KD], kexp_r[pp])
                if isin(b):
                    stand(sp, q2_r, b + 1)
                    if not early(b):
                        sp.wait_ge(st_r, QUADS * (b - 1))
                    apart(k.q2exp[par], k.q2[par], q2exp_r[par])
            load_ctx(0, 0)
            steps(sp, step)

        @block.gpsimd
        def _(pool):
            def step(b, m):
                par, p, pp, s = m % 2, b + 1, 1 - m % 2, b - 1
                if isin(p + 1):
                    rstd(pool, k, p + 1, par, var_r, rstd_r)
                if isin(s):
                    stand(pool, q2tr_r, s + 1)
                    pool.memset(r2(k.qpad[pp][:, :, NEGMAX:NEGMAX + 2]), 0.0).then_inc(rez_r, 1)
                if isin(p):
                    if not early(p):
                        stand(pool, ktr_r, p - 1)
                    stand(pool, kvc_r, p + 1)
                    src = k.kvraw[:, pp, 0:D]
                    if rope:
                        pool.tensor_tensor(src, src, k.bkv[:, 0:D], ALU.add).then_inc(bias_r, 1)
                        pool.wait_ge(bias_r, p + 1)
                        src = spin(pool, k, src, 0, kspin_r, 4 * p)
                    split(pool, k.kpad[pp], src, (0, 2), 1, khi_r, p, kpad_r)
                if isin(b):
                    if not early(b):
                        stand(pool, pv_r, QUADS * (b - 1))
                    heads = lambda t: t.rearrange("p (h d) -> p h d", d=HD)
                    v = heads(k.kvraw[:, par, D:2 * D])
                    if rope:
                        pool.tensor_tensor(k.vaug[par][:, :, 0:HD], v, heads(k.bkv[:, D:2 * D]), ALU.add).then_inc(vaug_r, 1)
                    else:
                        pool.tensor_copy(k.vaug[par][:, :, 0:HD], v).then_inc(vaug_r, 1)
                    pool.wait_ge(xn_r, b + 1)
                    pool.tensor_tensor(tile_of(k.x, b), tile_of(k.x, b), k.bo[n][:], ALU.add).then_inc(bo_r, 1)
                if isin(s) and n == 0:
                    for q in range(QUADS):
                        stand(pool, exp_r, QUADS * s + q + 1)
                        pool.affine_select(out=k.pt[q][:], in_=k.pt[q][:], compare_op=ALU.is_ge, fill=0.0, base=0,
                                           pattern=[[0, PER], [1, S]], channel_multiplier=-1).then_inc(prob_r, 1)
            rstd(pool, k, 0, 0, var_r, rstd_r)
            steps(pool, step)

        @block.scalar
        def _(act):
            def exps(s, quads):
                for q in quads:
                    act.wait_ge(st_r, QUADS * s + q + 1)
                    if not early(s, 1):
                        act.wait_ge(pv_r, QUADS * (s - 1) + q + 1)
                    act.activation(k.pt[q][:], ST[q % 2][:], ACT.Exp, scale=SCALE).then_inc(exp_r, 1)

            def step(b, m):
                par, p, pp, s, t = m % 2, b + 1, 1 - m % 2, b - 1, b - 2
                if isin(p):
                    act.wait_ge(kv_r, p + 1)
                    act.wait_ge(xt_r, p + 1)
                    if not early(p):
                        act.wait_ge(kpad_r, 2 * (p - 1))
                        act.wait_ge(vaug_r, p - 1)
                    act.activation(k.kvraw[:, pp, :], IN[:, 0:256], ACT.Copy).then_inc(kvc_r, 1)
                    if not early(p):
                        act.wait_ge(q_r, p - 1)
                    act.activation(k.xnT[:, pp, :], IN[:, 384:512], ACT.Copy).then_inc(xtc_r, 1)
                if isin(t):
                    act.wait_ge(pv_r, QUADS * (t + 1))
                    if not early(t):
                        act.wait_ge(otr_r, t - 1)
                    act.activation(k.pve[:, par, :], PV[:], ACT.Copy).then_inc(pvc_r, 1)
                if isin(p):
                    act.wait_ge(q_r, p + 1)
                    if not early(p):
                        act.wait_ge(qpad_r, 2 * (p - 1))
                    act.activation(k.qraw[:, pp, :], IN[:, 256:384], ACT.Copy).then_inc(qc_r, 1)
                    act.wait_ge(ktr_r, p + 1)
                    if not early(p, KD):
                        act.wait_ge(st_r, QUADS * (p - KD + 1))
                        act.wait_ge(kexp_r[pp], 32 * (p - pp))
                    act.activation(k.kd[(m + 1) % KD][:], TK[:], ACT.Copy).then_inc(kd_r, 1)
                if isin(s):
                    exps(s, (0, 1))
                if isin(t):
                    act.wait_ge(ot_r, t + 1)
                    if not early(t):
                        act.wait_ge(op_r, t - 1)
                    act.activation(k.ot[:, par, :], IN[:, 0:128], ACT.Copy).then_inc(otc_r, 1)
                if isin(s):
                    exps(s, (2, 3))
                if isin(b):
                    act.wait_ge(q2tr_r, b + 1)
                    if not early(b):
                        act.wait_ge(q2exp_r[par], 32 * (b - par))
                    act.activation(k.q2[par][:], TK[:], ACT.Copy).then_inc(q2_r, 1)
                if isin(p):
                    act.wait_ge(qtr_r, p + 1)
                    if not early(p):
                        act.wait_ge(s_r, QUADS * (p - 1))
                    act.activation(k.q1[pp][:], TQ[:], ACT.Copy).then_inc(q1_r, 1)
            steps(act, step)

        @block.vector
        def _(dve):
            def maxima(b, par, quads):
                for q in quads:
                    dve.wait_ge(s_r, QUADS * b + q + 1)
                    dve.tensor_reduce(k.negm[:, par, PER * q:PER * q + PER],
                                      SC[q % 2][:].rearrange("p (h s) -> p h s", s=S), AX.X, ALU.max,
                                      negate=True).then_inc(max_r, 1)

            def step(b, m):
                par, p, pp, t = m % 2, b + 1, 1 - m % 2, b - 2
                if isin(p + 1):
                    moments(dve, k, p + 1, par, stat_r, var_r)
                if isin(b):
                    maxima(b, par, (0, 1))
                if isin(t):
                    dve.wait_ge(otr_r, t + 1)
                    pv = TQ[:].rearrange("p (h d) -> p h d", d=SLOTS)
                    dve.reciprocal(k.rden[:, par, :], pv[:, :, HD]).then_inc(den_r, 1)
                    dve.wait_ge(den_r, t + 1)
                    if not early(t):
                        dve.wait_ge(ot_r, t - 1)
                    dve.tensor_tensor(k.on[:, par, :].rearrange("p (h d) -> p h d", d=HD), pv[:, :, 0:HD],
                                      k.rden[:, par, :].unsqueeze(2).broadcast_to([128, H, HD]), ALU.mult).then_inc(on_r, 1)
                if isin(b):
                    maxima(b, par, (2, 3))
                    dve.wait_ge(max_r, QUADS * (b + 1))
                    dve.wait_ge(qtr_r, b + 1)
                    slot = k.qpad[par][:, :, NEGMAX:NEGMAX + 2]
                    dve.tensor_copy(slot[:, :, 0], k.negm[:, par, :]).then_inc(slot0_r, 1)
                    dve.wait_ge(slot0_r, b + 1)
                    dve.tensor_tensor(slot[:, :, 1], k.negm[:, par, :], r2(slot[:, :, 0]), ALU.subtract)\
                       .then_inc(slot_r, 1)
                if isin(p):
                    dve.wait_ge(qc_r, p + 1)
                    if not early(p):
                        dve.wait_ge(rez_r, p - 1)
                    src = k.qraw[:, pp, :]
                    if rope:
                        dve.tensor_tensor(src, src, k.bq[:], ALU.add).then_inc(qbias_r, 1)
                        dve.wait_ge(qbias_r, p + 1)
                        src = spin(dve, k, src, 1, qspin_r, 4 * p)
                    split(dve, k.qpad[pp], src, (0, 1), 2, qhi_r, p, qpad_r)
                if isin(p + 1):
                    normed(dve, k, p + 1, par, k.xn[:, par, :], rstd_r, xn_r, xt_r, b + 1)
                if isin(t):
                    dve.wait_ge(op_r, t + 1)
                    dve.wait_ge(bo_r, t + 1)
                    xt = tile_of(k.x, t)
                    dve.tensor_tensor(xt, IN[:, 128:256], xt, ALU.add).then_inc(res_r, 1)
            norm(dve, k, 0, 0, k.xn[:, 0, :], stat_r, var_r, rstd_r, xn_r, None, 0)
            steps(dve, step)

        @block.tensor
        def _(pe):
            def step(b, m):
                par, p, pp, s, t = m % 2, b + 1, 1 - m % 2, b - 1, b - 2

                def pass1(quads):
                    for q in quads:
                        if not early(QUADS * b + q):
                            pe.wait_ge(max_r, QUADS * b + q - 1)
                        if n == 0:
                            pe.matmul(SC[q % 2][:], k.identb[:], k.mask_qk[:], start=True, stop=False,
                                      skip_group_check=True)
                        pe.matmul(SC[q % 2][:], k.q1[par][:, q, :], k.kexp[par][:, q, :, :], start=n == 1,
                                  stop=True, skip_group_check=n == 0).then_inc(s_r, 1)

                def pass2(quads):
                    for q in quads:
                        if not early(QUADS * s + q):
                            pe.wait_ge(exp_r, QUADS * s + q - 1)
                        pe.matmul(ST[q % 2][:], k.kd[(m - 1) % KD][:, q, :], k.q2exp[pp][:, q, :, :], start=True,
                                  stop=True).then_inc(st_r, 1)
                if isin(p):
                    pe.wait_ge(ctx_in[pp], 8 * (p - pp) + 16)
                    if not early(p, 1):
                        pe.wait_ge(qc_r, p)
                    if not early(t, 1):
                        pe.wait_ge(res_r, t)
                    pe.matmul(IN[:, 0:256], k.ctxc[:, pp, :], k.wkv[n][:], start=True, stop=True).then_inc(kv_r, 1)
                    pe.wait_ge(xn_r, p + 1)
                    pe.transpose(IN[:, 384:512], k.xn[:, pp, :], k.ident[:]).then_inc(xt_r, 1)
                if isin(t):
                    pe.wait_ge(vaug_r, t + 1)
                    if not early(t, 1):
                        pe.wait_ge(pvc_r, t)
                    for q in range(QUADS):
                        pe.wait_ge(prob_r, QUADS * t + q + 1)
                        for j in range(PER):
                            mm = pe.matmul(PV[SLOTS * j:SLOTS * (j + 1), q * S:q * S + S],
                                           k.vaug[par][:, PER * q + j, :], k.pt[q][:, j, :], start=True, stop=True)
                        mm.then_inc(pv_r, 1)
                if isin(b):
                    pe.wait_ge(kexp_r[par], 32 * (b - par) + 64)
                    pe.wait_ge(q1_r, b + 1)
                    pass1((0, 1))
                if isin(p):
                    pe.wait_ge(kvc_r, p + 1)
                    pe.wait_ge(xtc_r, p + 1)
                    pe.matmul(IN[:, 256:384], k.xnT[:, pp, :], k.wq[n][:], start=True, stop=True).then_inc(q_r, 1)
                if isin(t):
                    pe.wait_ge(pvc_r, t + 1)
                    if isin(b):
                        pe.wait_ge(q1_r, b + 1)
                    for q in range(QUADS):
                        mm = pe.transpose(TQ[:, q * S:q * S + S], k.pve[:, par, q * S:q * S + S], k.ident[:])
                    mm.then_inc(otr_r, 1)
                if isin(p):
                    pe.wait_ge(kpad_r, 2 * (p + 1))
                    if isin(s):
                        pe.wait_ge(q2_r, s + 1)
                    turn(pe, TK, k.kpad[pp], k.identr, ktr_r)
                if isin(b):
                    pass1((2, 3))
                if isin(s):
                    pe.wait_ge(q2exp_r[pp], 32 * (s - pp) + 64)
                    pass2((0, 1))
                if isin(t):
                    pe.wait_ge(on_r, t + 1)
                    if isin(p):
                        pe.wait_ge(qc_r, p + 1)
                    elif not early(t, 1):
                        pe.wait_ge(res_r, t)
                    pe.transpose(IN[:, 0:128], k.on[:, par, :], k.ident[:]).then_inc(ot_r, 1)
                if isin(s):
                    pass2((2, 3))
                if isin(t):
                    pe.wait_ge(otc_r, t + 1)
                    pe.matmul(IN[:, 128:256], k.ot[:, par, :], k.wo[n][:], start=True, stop=True).then_inc(op_r, 1)
                if isin(b):
                    pe.wait_ge(slot_r, b + 1)
                    if isin(p):
                        pe.wait_ge(kd_r, p + 1)
                    elif isin(s):
                        pe.wait_ge(q2_r, s + 1)
                    turn(pe, TK, k.qpad[par], k.identr, q2tr_r)
                if isin(p):
                    pe.wait_ge(qpad_r, 2 * (p + 1))
                    if isin(t):
                        pe.wait_ge(on_r, t + 1)
                    turn(pe, TQ, k.qpad[pp], k.identr, qtr_r)
            steps(pe, step)


def turn(pe, bank, pad, identr, done):
    for q in range(QUADS):
        mm = pe.matmul(bank[:, q * S:q * S + S], pad[:, PER * q:PER * q + PER, :], identr[:], start=True, stop=True)
    mm.then_inc(done, 1)


def split(eng, pad, src, hi, lo, first, count, done):
    s3 = src.rearrange("p (h d) -> p h d", d=HD)
    at = lambda n: pad[:, :, n * HD:n * HD + HD]
    eng.tensor_copy(at(hi[0]), s3).then_inc(first, 1)
    stand(eng, first, count + 1)
    eng.tensor_copy(at(hi[1]), r2(at(hi[0]))).then_inc(done, 1)
    eng.tensor_tensor(at(lo), s3, r2(at(hi[0])), ALU.subtract).then_inc(done, 1)


def spin(eng, k, src, which, sem, count):
    t1, t2 = k.rt[:, which, 0, :], k.rt[:, which, 1, :]
    v = lambda x: x.rearrange("p (h d) -> p h d", d=HD)
    half = HD // 2
    cos = k.rope[:, 0:1, :].broadcast_to([128, H, HD])
    sin = k.rope[:, 1:2, :]
    eng.tensor_tensor(v(t1), v(src), cos, ALU.mult).then_inc(sem, 1)
    eng.tensor_tensor(v(t2)[:, :, 0:half], v(src)[:, :, half:HD], sin[:, :, 0:half].broadcast_to([128, H, half]),
                      ALU.mult).then_inc(sem, 1)
    eng.tensor_tensor(v(t2)[:, :, half:HD], v(src)[:, :, 0:half], sin[:, :, half:HD].broadcast_to([128, H, half]),
                      ALU.mult).then_inc(sem, 1)
    eng.wait_ge(sem, count + 3)
    eng.tensor_tensor(t1, t1, t2, ALU.add).then_inc(sem, 1)
    stand(eng, sem, count + 4)
    return t1


def tile_of(t, b):
    return t[:, b, :] if isinstance(b, int) else t[:, bass.ds(b, 1), :].rearrange("p a d -> p (a d)")


def rstd(pool, k, b, par, var_r, rstd_r):
    stand(pool, var_r, b + 1)
    pool.tensor_scalar(k.rstd[:, par, :], k.mv[:, par, 1:2], EPS, None, ALU.add).then_inc(rstd_r, 1)
    pool.wait_ge(rstd_r, 2 * b + 1)
    pool.tensor_tensor(k.rstd[:, par, :], k.rstd[:, par, :], k.mhalf[:, 0:1], ALU.pow).then_inc(rstd_r, 1)


def moments(dve, k, b, par, stat_r, var_r):
    dve.bn_stats(k.stat[:, par, :], tile_of(k.x, b)).then_inc(stat_r, 1)
    stand(dve, stat_r, b + 1)
    dve.bn_aggr(k.mv[:, par, :], k.stat[:, par, :]).then_inc(var_r, 1)


def normed(dve, k, b, par, out, rstd_r, xn_r, used, used_at):
    dve.wait_ge(rstd_r, 2 * (b + 1))
    if used is not None and not (isinstance(b, int) and b < 2):
        dve.wait_ge(used, used_at)
    dve.tensor_scalar(out, tile_of(k.x, b), k.mv[:, par, 0:1], k.rstd[:, par, :],
                      ALU.subtract, ALU.mult).then_inc(xn_r, 1)


def norm(dve, k, b, par, out, stat_r, var_r, rstd_r, xn_r, used, used_at):
    moments(dve, k, b, par, stat_r, var_r)
    normed(dve, k, b, par, out, rstd_r, xn_r, used, used_at)


def normed_tiles(nc, k, n):
    ffn_room(k)
    sem = lambda s: k.sem(f"N{n}_{s}")
    TRB, HRB, LGB = k.bank[0], k.bank[1], k.bank[2:4]
    (stat_r, var_r, rstd_r, t_r, kept_r, tt_r, ttc_r, hr_r, hrc_r, lg_r, lgc_r, copied_r) = map(sem, (
        "stat", "var", "rstd", "t", "kept", "tT", "tT_copied", "hr", "hr_silu", "logits", "logits_out", "copied"))
    E = E1 if n else E0

    def early(b, by=2):
        return isinstance(b, int) and b < by

    def steps(eng, step):
        for b in range(2):
            step(b, b)
        with eng.Fori(1, B // 2) as i:
            for par in range(2):
                step(i * 2 + par, par)

    with nc.Block() as block:
        @block.gpsimd
        def _(pool):
            def step(b, par):
                rstd(pool, k, b, par, var_r, rstd_r)
                if n:
                    pool.tensor_copy(tile_of(k.var, b), k.mv[:, par, 1:2]).then_inc(kept_r, 1)
                    stand(pool, ttc_r, b + 1)
                    pool.tensor_copy(tile_of(k.tT, b), k.xnT[:, par, :]).then_inc(copied_r, 1)
                else:
                    pool.wait_ge(t_r, b + 1)
                    pool.tensor_tensor(tile_of(k.x, b), tile_of(k.x, b), k.xn[:, par, :], ALU.add).then_inc(kept_r, 1)
            steps(pool, step)

        @block.vector
        def _(dve):
            def logits_out(b, par):
                dve.wait_ge(lg_r, b + 1)
                dve.tensor_copy(tile_of(k.lg[n], b), LGB[par][:, 0:E]).then_inc(lgc_r, 1)

            def step(b, par):
                if not early(b):
                    dve.wait_ge(kept_r, b - 1)
                norm(dve, k, b, par, k.xn[:, par, :], stat_r, var_r, rstd_r, t_r, tt_r, b - 1)
                if not early(b, 1):
                    logits_out(b - 1, 1 - par)
            steps(dve, step)
            logits_out(B - 1, 1)

        @block.scalar
        def _(act):
            def step(b, par):
                act.wait_ge(tt_r, b + 1)
                if not early(b):
                    act.wait_ge(lg_r, b - 1)
                    if n:
                        act.wait_ge(copied_r, b - 1)
                act.activation(k.xnT[:, par, :], TRB[:, 0:S], ACT.Copy).then_inc(ttc_r, 1)
                if not n:
                    act.activation(tile_of(k.tT, b), TRB[:, 0:S], ACT.Copy).then_inc(copied_r, 1)
                    act.wait_ge(hr_r, b + 1)
                    act.activation(k.ot[:, par, :], HRB[:, 0:S], ACT.Silu, bias=k.rb1[:]).then_inc(hrc_r, 1)
            steps(act, step)

        @block.tensor
        def _(pe):
            def step(b, par):
                pe.wait_ge(t_r, b + 1)
                if not early(b, 1):
                    pe.wait_ge(ttc_r if n else copied_r, b)
                pe.transpose(TRB[:, 0:S], k.xn[:, par, :], k.ident[:]).then_inc(tt_r, 1)
                pe.wait_ge(ttc_r, b + 1)
                if n:
                    if not early(b):
                        pe.wait_ge(lgc_r, b - 1)
                    pe.matmul(LGB[par][:, 0:E], k.xnT[:, par, :], k.sn[:], start=True, stop=True).then_inc(lg_r, 1)
                    return
                if not early(b, 1):
                    pe.wait_ge(hrc_r, b)
                pe.matmul(HRB[:, 0:S], k.rw1[:], k.xnT[:, par, :], start=True, stop=True).then_inc(hr_r, 1)
                pe.wait_ge(hrc_r, b + 1)
                if not early(b):
                    pe.wait_ge(lgc_r, b - 1)
                pe.matmul(LGB[par][:, 0:E], k.ot[:, par, :], k.rw2[:], start=True, stop=False)
                pe.matmul(LGB[par][:, 0:E], k.ones_row[:], k.rb2[:], start=False, stop=True).then_inc(lg_r, 1)
            steps(pe, step)


def routing(nc, k, n):
    sem = lambda s: k.sem(f"R{n}_{s}")
    E = E1 if n else E0
    lg, ex, sel, tmp, mx, idx = k.lg[n], k.ex[:, :, 0:E], k.sel[:, :, 0:E], k.tmp[:, :, 0:E], k.mx, k.idx
    chain_v, chain_p, for_pool, pooled, for_exp, exped, wpad_r, turned, out_r = map(sem, (
        "dve", "pool", "for_pool", "pooled", "for_exp", "exped", "wpad", "turned", "wT"))
    wide = lambda x: x.unsqueeze(2).broadcast_to([128, B, E])
    with nc.Block() as block:
        @block.gpsimd
        def _(pool):
            link = chain(pool, chain_p)
            link(pool.memset(r2(k.wpad[:]), 0.0))
            if n:
                v, r = k.var[:, :, 0], k.rn[:, 0, :]
                link(pool.tensor_scalar(r, v, EPS, None, ALU.add))
                link(pool.tensor_tensor(r, r, k.mhalf[:], ALU.pow))
                link(pool.tensor_tensor(r, r, r, ALU.mult))
                link(pool.tensor_tensor(r, r, v, ALU.mult))
                link(pool.tensor_scalar(r, r, float(D), TINY, ALU.mult, ALU.max))
                link(pool.tensor_tensor(r, r, k.mhalf[:], ALU.pow))
            pool.engine_nop().then_inc(pooled, 1)

        @block.vector
        def _(dve):
            link = chain(dve, chain_v)
            dve.wait_ge(pooled, 1)
            if n:
                link(dve.tensor_tensor(lg[:], lg[:], wide(k.rn[:, 0, :]), ALU.mult))
                link(dve.tensor_tensor(lg[:], lg[:], k.sig[:].unsqueeze(1).broadcast_to([128, B, E]), ALU.subtract))
            for b in range(B):
                link(dve.max(mx[:, b, :], lg[:, b, :]))
                link(dve.max_index(idx[:, b, :], mx[:, b, :], lg[:, b, :]))
            iota = k.iota[:, 0:E].unsqueeze(1).broadcast_to([128, B, E])
            link(dve.tensor_tensor(sel, iota, wide(idx[:, :, 0]), ALU.is_equal))
            link(dve.tensor_tensor(tmp, iota, wide(idx[:, :, 1]), ALU.is_equal))
            link(dve.tensor_tensor(sel, sel, tmp, ALU.add))
            top = mx[:, :, 0]
            if n:
                link(dve.tensor_scalar(k.rn[:, 1, :], top, 0.0, None, ALU.is_le))
                link(dve.tensor_tensor(sel, sel, wide(k.rn[:, 1, :]), ALU.mult))
                link(dve.tensor_scalar(tmp, lg[:], 0.0, None, ALU.is_gt))
                link(dve.tensor_tensor(sel, sel, tmp, ALU.add))
                link(dve.tensor_scalar(lg[:], lg[:], 0.0, None, ALU.max))
                link(dve.tensor_scalar(k.rn[:, 1, :], top, 0.0, None, ALU.max))
                top = k.rn[:, 1, :]
            dve.tensor_tensor(ex, lg[:], wide(top), ALU.subtract).then_inc(for_exp, 1)
            dve.wait_ge(exped, 1)
            link(dve.tensor_tensor(ex, ex, sel, ALU.mult))
            link(dve.tensor_reduce(k.rn[:, 1, :], ex, AX.X, ALU.add))
            link(dve.reciprocal(k.rn[:, 1, :], k.rn[:, 1, :]))
            link(dve.tensor_tensor(ex, ex, wide(k.rn[:, 1, :]), ALU.mult))
            link(dve.tensor_copy(k.wpad[:, :, 0:E], ex))
            dve.tensor_tensor(k.wpad[:, :, E:2 * E], ex, r2(k.wpad[:, :, 0:E]), ALU.subtract).then_inc(wpad_r, 1)

        @block.scalar
        def _(act):
            act.wait_ge(for_exp, 1)
            act.activation(ex, ex, ACT.Exp).then_inc(exped, 1)
            for g in range(G):
                act.wait_ge(turned, g + 1)
                act.activation(k.wT[:, g * GW:(g + 1) * GW], k.bank[g][:], ACT.Copy).then_inc(out_r, 1)

        @block.tensor
        def _(pe):
            pe.wait_ge(wpad_r, 1)
            for g in range(G):
                for t in range(GT):
                    mm = pe.matmul(k.bank[g][:, t * S:t * S + S], k.wpad[:, g * GT + t, :], k.identr[:],
                                   start=True, stop=True)
                mm.then_inc(turned, 1)


CREDIT = 3


def experts0(nc, k):
    sem = lambda s: k.sem(f"X0_{s}")
    WB, U, Y, T = k.bank[0:2], k.bank[2:4], k.bank[4], k.bank[5]
    wb_r, u_r, silu_r, hw_r, down_r, y_r, yc_r, yt_r, res_r = map(sem, (
        "wB", "up", "silu", "hw", "down", "y", "y_copied", "yT", "residual"))
    N = E0 * HC
    with nc.Block() as block:
        @block.vector
        def _(dve):
            dve.sem_inc(hw_r, CREDIT)
            dve.sem_inc(res_r, CREDIT)
            with dve.Fori(0, G) as g:
                for e in range(E0):
                    dve.wait_ge(wb_r, g * E0 + e + 1)
                    for c in range(HC):
                        v = HC * e + c
                        dve.wait_ge(silu_r, g * N + v + 1 + CREDIT)
                        dve.wait_ge(down_r, g * N + v - 1 + CREDIT)
                        dve.tensor_tensor(k.hw[c][:], k.hs[c][:], WB[e % 2][:], ALU.mult).then_inc(hw_r, 1)
                dve.wait_ge(yt_r, g + 1)
                xg = k.x[:, bass.ds(g * GT, GT), :]
                dve.tensor_tensor(xg, T[:].rearrange("p (t d) -> p t d", d=D), xg, ALU.add).then_inc(res_r, 1)

        @block.scalar
        def _(act):
            act.sem_inc(silu_r, CREDIT)
            with act.Fori(0, G) as g:
                for e in range(E0):
                    for c in range(HC):
                        v = HC * e + c
                        act.wait_ge(u_r, g * N + v + 1)
                        act.wait_ge(hw_r, g * N + v - 1 + CREDIT)
                        act.activation(k.hs[c][:], U[c][:], ACT.Silu, bias=k.eb1[:, e, c:c + 1]).then_inc(silu_r, 1)
                act.wait_ge(y_r, g + 1)
                act.activation(k.yT[:], Y[:], ACT.Copy).then_inc(yc_r, 1)

        @block.tensor
        def _(pe):
            pe.sem_inc(down_r, CREDIT)
            with pe.Fori(0, G) as g:
                tT = k.tT[:, bass.ds(g * GT, GT), :]
                wT = k.wT[:, bass.ds(g * GW, GW)]

                def down(e):
                    for c in range(HC):
                        v = HC * e + c
                        pe.wait_ge(hw_r, g * N + v + 1 + CREDIT)
                        mm = pe.matmul(Y[:], k.ew2[:, e, c, :], k.hw[c][:], start=False, stop=v == N - 1)
                        mm.then_inc(down_r, 1)
                pe.wait_ge(res_r, g + CREDIT)
                pe.matmul(Y[:], k.eb2[0:2 * E0, :], r2(k.wT[0:2 * E0, bass.ds(g * GW, GW)]), start=True, stop=False)
                for e in range(E0):
                    pe.wait_ge(hw_r, g * N + HC * e - 2 + CREDIT)
                    pe.matmul(WB[e % 2][:], k.sel0[:, e, :], wT, start=True, stop=True).then_inc(wb_r, 1)
                    for c in range(HC):
                        v = HC * e + c
                        pe.wait_ge(silu_r, g * N + v - 1 + CREDIT)
                        pe.matmul(U[c][:], k.ew1[:, e, c * 128:(c + 1) * 128], tT, start=True, stop=True)\
                          .then_inc(u_r, 1)
                    if e:
                        down(e - 1)
                down(E0 - 1)
                pe.wait_ge(down_r, g * N + N + CREDIT)
                pe.sem_inc(y_r, 1)
                pe.wait_ge(yc_r, g + 1)
                for t in range(GT):
                    mm = pe.transpose(T[:, t * S:t * S + S], k.yT[:, t * S:t * S + S], k.ident[:])
                mm.then_inc(yt_r, 1)


def experts1(nc, k, a):
    sem = lambda s: k.sem(f"X1_{s}")
    QKV, WB, A, M, O = k.bank[0:3], k.bank[3:5], k.bank[5], k.bank[6], k.bank[7]
    (wb_r, z_r, used_r, qkv_r, qkvc_r, s_r, max_r, nms_r, exp_r, sum_r, p_r, pt_r, ptc_r, vn_r, vnc_r, o_r, oc_r,
     oT_r, oTc_r, out_r, put_r, sent_r) = map(sem, (
        "wB", "z", "z_used", "qkv", "qkv_copied", "scores", "max", "neg_max", "exp", "sum", "probs", "probsT",
        "probsT_copied", "v_turned", "v_copied", "o", "o_copied", "outT", "outT_copied", "out", "out_put", "sent"))
    N = 2 * E1
    with nc.Block() as block:
        @block.sync
        def _(sp):
            with sp.Fori(0, G) as g:
                stand(sp, put_r, g + 1)
                sp.dma_start(a["out"][:, bass.ds(g * GT, GT), :], k.x[:, bass.ds(g * GT, GT), :]).then_inc(sent_r, 16)
            sp.wait_ge(sent_r, 16 * G)

        @block.vector
        def _(dve):
            dve.sem_inc(z_r, CREDIT)
            dve.sem_inc(max_r, CREDIT)
            with dve.Fori(0, G) as g:
                def scaled(src, first):
                    for e in range(E1):
                        v = first + e
                        dve.wait_ge(wb_r, g * N + v + 1)
                        dve.wait_ge(used_r, g * N + v - 1 + CREDIT)
                        dve.tensor_tensor(k.hw[v % 2][:], src, WB[v % 2][:], ALU.mult).then_inc(z_r, 1)
                scaled(k.tT[:, bass.ds(g * GT, GT), :].rearrange("p t s -> p (t s)"), 0)
                dve.wait_ge(s_r, g + 1)
                dve.tensor_reduce(k.nm4[:, 0:GT], A[:].rearrange("p (t s) -> p t s", s=S), AX.X, ALU.max,
                                  negate=True).then_inc(max_r, 1)
                dve.wait_ge(max_r, g + 1 + CREDIT)
                dve.tensor_scalar(k.nm4[:, 0:GT], k.nm4[:, 0:GT], SCALE1, None, ALU.mult).then_inc(nms_r, 1)
                dve.wait_ge(exp_r, GT * (g + 1))
                dve.reciprocal(k.nm4[:, 2 * GT:3 * GT], k.nm4[:, GT:2 * GT]).then_inc(sum_r, 1)
                dve.wait_ge(sum_r, g + 1)
                p3 = k.hs[0][:].rearrange("p (t s) -> p t s", s=S)
                dve.tensor_tensor(p3, p3, k.nm4[:, 2 * GT:3 * GT].unsqueeze(2).broadcast_to([128, GT, S]), ALU.mult)\
                   .then_inc(p_r, 1)
                dve.wait_ge(o_r, g + 1)
                dve.tensor_copy(k.oT[:], A[:]).then_inc(oc_r, 1)
                dve.wait_ge(oc_r, g + 1)
                scaled(k.oT[:], E1)
                dve.wait_ge(out_r, g + 1)
                xg = k.x[:, bass.ds(g * GT, GT), :]
                dve.tensor_tensor(xg, A[:].rearrange("p (t d) -> p t d", d=D), xg, ALU.add).then_inc(put_r, 1)

        @block.scalar
        def _(act):
            with act.Fori(0, G) as g:
                act.wait_ge(qkv_r, g + 1)
                for n in range(3):
                    act.activation(k.qkv[n][:], QKV[n][:], ACT.Copy).then_inc(qkvc_r, 1)
                act.wait_ge(vn_r, g + 1)
                act.activation(k.hs[1][:], M[:], ACT.Copy).then_inc(vnc_r, 1)
                act.wait_ge(nms_r, g + 1)
                for t in range(GT):
                    act.activation(k.hs[0][:, t * S:t * S + S], A[:, t * S:t * S + S], ACT.Exp, scale=SCALE1,
                                   bias=k.nm4[:, t:t + 1], accum_out=k.nm4[:, GT + t:GT + t + 1]).then_inc(exp_r, 1)
                act.wait_ge(pt_r, g + 1)
                act.activation(k.yT[:], M[:], ACT.Copy).then_inc(ptc_r, 1)
                act.wait_ge(oT_r, g + 1)
                act.activation(k.yT[:], O[:], ACT.Copy).then_inc(oTc_r, 1)

        @block.tensor
        def _(pe):
            pe.sem_inc(used_r, CREDIT)
            with pe.Fori(0, G) as g:
                wT = k.wT[:, bass.ds(g * GW, GW)]
                tile = lambda x, t: x[:, t * S:t * S + S]

                def weights(v):
                    pe.wait_ge(z_r, g * N + v - 2 + CREDIT)
                    pe.matmul(WB[v % 2][:], k.sel1[:, v % E1, :], wT, start=True, stop=True).then_inc(wb_r, 1)

                def experts(first, banks, projs):
                    weights(first)
                    for e in range(E1):
                        if e + 1 < E1:
                            weights(first + e + 1)
                        pe.wait_ge(z_r, g * N + first + e + 1 + CREDIT)
                        for bank, proj in zip(banks, projs):
                            mm = pe.matmul(bank[:], proj[:, e, :], k.hw[(first + e) % 2][:], start=e == 0, stop=e == E1 - 1)
                        mm.then_inc(used_r, 1)

                experts(0, QKV, k.p1[0:3])
                pe.wait_ge(used_r, g * N + E1 + CREDIT)
                pe.sem_inc(qkv_r, 1)
                pe.wait_ge(qkvc_r, 3 * (g + 1))
                for t in range(GT):
                    mm = pe.matmul(tile(A, t), tile(k.qkv[0], t), tile(k.qkv[1], t), start=True, stop=True)
                mm.then_inc(s_r, 1)
                for t in range(GT):
                    mm = pe.transpose(tile(M, t), tile(k.qkv[2], t), k.ident[:])
                mm.then_inc(vn_r, 1)
                pe.wait_ge(p_r, g + 1)
                pe.wait_ge(vnc_r, g + 1)
                for t in range(GT):
                    mm = pe.transpose(tile(M, t), tile(k.hs[0], t), k.ident[:])
                mm.then_inc(pt_r, 1)
                pe.wait_ge(ptc_r, g + 1)
                for t in range(GT):
                    mm = pe.matmul(tile(A, t), tile(k.hs[1], t), tile(k.yT, t), start=True, stop=True)
                mm.then_inc(o_r, 1)
                experts(E1, [O], [k.p1[3]])
                pe.wait_ge(used_r, g * N + N + CREDIT)
                pe.sem_inc(oT_r, 1)
                pe.wait_ge(oTc_r, g + 1)
                for t in range(GT):
                    mm = pe.transpose(tile(A, t), tile(k.yT, t), k.ident[:])
                mm.then_inc(out_r, 1)


def store(nc, k, a):
    s_out = k.sem("out")
    with nc.Block() as block:
        @block.sync
        def _(sp):
            sp.dma_start(a["out"], k.x[:]).then_inc(s_out, 16)
            sp.wait_ge(s_out, 16)


STAGES = [[lambda nc, k, a: attention(nc, k, a, 0)],
          [lambda nc, k, a: normed_tiles(nc, k, 0), lambda nc, k, a: routing(nc, k, 0), lambda nc, k, a: experts0(nc, k)],
          [lambda nc, k, a: attention(nc, k, a, 1)],
          [lambda nc, k, a: normed_tiles(nc, k, 1), lambda nc, k, a: routing(nc, k, 1),
           lambda nc, k, a: experts1(nc, k, a)]]
PHASES = sum(STAGES, [])


def program(nc, a):
    with ExitStack() as ctx:
        k = Core(nc, ctx)
        k.phase(setup, a)
        for p in PHASES:
            k.phase(p, a)
        if PHASES[-1] is not STAGES[-1][-1]:
            k.phase(store, a)
        k.rooms.close()


def host(inputs):
    f = lambda x: np.ascontiguousarray(np.asarray(x))
    i = {n: np.asarray(v) for n, v in inputs.items()}
    o = {"x": i["x"].transpose(1, 0, 2), "ctxT": i["ctx_1024"].transpose(2, 0, 1).reshape(D, B * S)}
    for n, (q, kk, v, w, bo) in enumerate((("L0_xattn_WQ", "L0_xattn_WK", "L0_xattn_WV", "L0_xattn_WO", "L0_xattn_bO"),
                                    ("L1_xattn_Wq", "L1_xattn_Wk", "L1_xattn_Wv", "L1_xattn_Wo", "L1_xattn_bo"))):
        o |= {f"wqT{n}": i[q].T, f"wkT{n}": i[kk].T, f"wvT{n}": i[v].T, f"woT{n}": i[w].T, f"bo{n}": i[bo].reshape(D)}
    o |= {"bq": i["L1_xattn_bq"].reshape(D), "bk": i["L1_xattn_bk"].reshape(D), "bv": i["L1_xattn_bv"].reshape(D)}
    for n in ("rw1", "rb1", "rw2", "ew1", "eb1", "ew2", "eb2"):
        o[n] = i["L0_ffn_" + n]
    o["rb2"] = i["L0_ffn_rb2"].reshape(1, E0)
    o["rb1"] = o["rb1"].reshape(D, 1)
    o["ew1"] = o["ew1"].transpose(1, 0, 2)
    o["eb1"] = o["eb1"].reshape(E0, HC, 128).transpose(2, 0, 1)
    o["ew2"] = o["ew2"].reshape(E0, HC, 128, D).transpose(2, 0, 1, 3)
    o["sim"], o["gates"] = i["L1_ffn_sim_matrix"], i["L1_ffn_gates"]
    for n, p in enumerate("qkvo"):
        o[f"proj{n}"] = i[f"L1_ffn_{p}_proj"].transpose(1, 0, 2)
    o["c_ident"] = np.eye(128, dtype=np.float32)
    o["c_iota"] = np.tile(np.arange(E1, dtype=np.float32), (128, 1))
    ang = 2.0 * np.outer(np.arange(S), 1.0 / 10000.0 ** (np.arange(0, HD, 2) / HD))
    cos, sin = np.cos(ang), np.sin(ang)
    o["c_rope"] = np.stack([np.concatenate([cos, cos], 1), np.concatenate([-sin, sin], 1)], 1).astype(np.float32)
    qk = np.where(np.tril(np.ones((S, S), bool)), 0.0, -1e30).astype(np.float32)
    o["c_mask"] = np.tile(qk, (1, PER))
    sel = []
    for n, e in ((E0, 8), (E1, 16)):
        m = np.zeros((128, n, 128), np.float32)
        for e in range(n):
            m[e, e], m[e + n, e] = 1.0, 1.0
        sel.append(m.reshape(128, -1))
    o["c_sel"] = np.concatenate(sel, 1)
    return {n: f(v) for n, v in o.items()}




def kernel(**inputs):
    import concourse.bacc as bacc
    from concourse.bass_utils import run_bass_kernel_spmd

    nc = bacc.Bacc("TRN2", target_bir_lowering=False, num_devices=1)
    arrays = host(inputs)
    a = {n: nc.dram_tensor(f"in_{n}", v.shape, mybir.dt.from_np(v.dtype), kind="ExternalInput").ap()
         for n, v in arrays.items()}
    a["out"] = nc.dram_tensor("out_y", (S, B, D), F32, kind="ExternalOutput").ap()
    program(nc, a)
    r = run_bass_kernel_spmd(nc, [{f"in_{n}": v for n, v in arrays.items()}], core_ids=[0])
    return r.results[0]["out_y"].transpose(1, 0, 2)
```
